# Optimizing a Trainium2 kernel written in Bass

```python
import numpy as np
import jax
import jax.numpy as jnp

def _softmax(x, axis=-1):
    return jax.nn.softmax(x, axis=axis)

def _gelu(x):
    return jax.nn.gelu(x, approximate=True)

def _silu(x):
    return jax.nn.silu(x)

def _sigmoid(x):
    return jax.nn.sigmoid(x)

def _layernorm(x, axis=-1, eps=1e-05):
    m = jnp.mean(x, axis=axis, keepdims=True)
    v = jnp.var(x, axis=axis, keepdims=True)
    return (x - m) / jnp.sqrt(v + eps)

def _scatter_add(tgt, idx, src, axis=0):
    return tgt.at[idx].add(src)

def _segment_sum(src, seg, n):
    return jax.ops.segment_sum(src, seg, n)
kernel_name = 'mk_adj_preln_d2_adj_r2_0f9d6b'

def setup_inputs(seed: int=0):
    np.random.seed(seed)
    _w = jnp.asarray

    def _rec_inputs():
        import jax
        import jax.numpy as jnp
        _gk = jax.random.key(seed)
        x = -0.0003929 + 0.9999 * jax.random.normal(jax.random.fold_in(_gk, 1), (8, 1024, 256), jnp.float32)
        _w = (1.0 + jnp.arange(1024, dtype=jnp.float32)) ** (-0.5)
        _w = _w / _w.mean()
        _pij = jnp.clip(0.00195312 * _w[:, None] * _w[None, :], 0.0, 1.0)
        _a = jax.random.uniform(jax.random.fold_in(_gk, 2), (1024, 1024)) < _pij
        _a = jnp.logical_or(_a, jnp.swapaxes(_a, -1, -2))
        _a = jnp.logical_or(_a, jnp.eye(1024, dtype=bool))
        _af = _a.astype(jnp.float32)
        _af = _af * jax.random.uniform(jax.random.fold_in(_gk, 3), (1024, 1024), jnp.float32, 0.05, 1)
        adj = _af
        return (x, adj)
    x, adj = _rec_inputs()

    def _L0_gnn_setup():
        import jax, jax.numpy as jnp
        import numpy as np
        B, N, F_IN, F_OUT = (16, 1024, 256, 256)
        key = jax.random.key(seed)
        k1, k2, k3 = jax.random.split(key, 3)
        x = jax.random.normal(k1, (B, N, F_IN), dtype=jnp.float32)
        adj = jax.random.uniform(k2, (N, N), dtype=jnp.float32)
        bound = np.sqrt(6.0 / F_OUT)
        weight = jax.random.uniform(k3, (F_IN, F_OUT), dtype=jnp.float32, minval=-bound, maxval=bound)
        bias = jnp.zeros((F_OUT,), dtype=jnp.float32)
        return {'x': x, 'adj': adj, 'weight': weight, 'bias': bias}
    _L0_gnn_all = _L0_gnn_setup()
    _L0_gnn_in = {k: v for k, v in _L0_gnn_all.items() if k in ('weight', 'bias')}
    del _L0_gnn_all

    def _L1_gnn_setup():
        import jax, jax.numpy as jnp
        import numpy as np
        ALPHA = 0.2
        key = jax.random.key(seed)
        k0, k1, k2, k3 = jax.random.split(key, 4)
        B, N, C, F = (64, 512, 256, 256)
        x = jax.random.normal(k0, (B, N, C), dtype=jnp.float32)
        W = jax.random.normal(k1, (C, F), dtype=jnp.float32) * (1.414 / np.sqrt(C + F))
        a = jax.random.normal(k2, (2 * F, 1), dtype=jnp.float32) * (1.414 / np.sqrt(2 * F + 1))
        beta = jnp.ones((1,), dtype=jnp.float32)
        mask = (jax.random.uniform(k3, (N, N)) < 0.3).astype(jnp.float32)
        return {'x': x, 'W': W, 'a': a, 'beta': beta, 'mask': mask}
    _L1_gnn_all = _L1_gnn_setup()
    _L1_gnn_in = {k: v for k, v in _L1_gnn_all.items() if k in ('W', 'a', 'beta')}
    del _L1_gnn_all
    return {'x': x, 'adj': adj, 'L0_gnn_weight': _L0_gnn_in['weight'], 'L0_gnn_bias': _L0_gnn_in['bias'], 'L1_gnn_W': _L1_gnn_in['W'], 'L1_gnn_a': _L1_gnn_in['a'], 'L1_gnn_beta': _L1_gnn_in['beta']}

def reference(x, adj, L0_gnn_weight, L0_gnn_bias, L1_gnn_W, L1_gnn_a, L1_gnn_beta):
    import jax
    import jax.numpy as jnp

    def _L0_gnn_ref(x, adj, weight, bias):
        import jax, jax.numpy as jnp
        import numpy as np
        B, N, F_IN, F_OUT = (16, 1024, 256, 256)
        deg = adj.sum(axis=1)
        deg_inv_sqrt = jnp.where(deg > 0, jax.lax.rsqrt(deg), 0.0)
        norm_adj = adj * deg_inv_sqrt[:, None] * deg_inv_sqrt[None, :]
        support = jnp.einsum('bni,io->bno', x, weight)
        output = jnp.einsum('nm,bmo->bno', norm_adj, support)
        return output + bias

    def _L1_gnn_ref(x, W, a, beta, mask):
        import jax, jax.numpy as jnp
        import numpy as np
        ALPHA = 0.2
        F_ = W.shape[1]
        h = jnp.einsum('bnc,cf->bnf', x, W)
        a1, a2 = (a[:F_, 0], a[F_:, 0])
        s1 = jnp.einsum('bnf,f->bn', h, a1)
        s2 = jnp.einsum('bnf,f->bn', h, a2)
        e = jax.nn.leaky_relu(s1[:, :, None] + s2[:, None, :], negative_slope=ALPHA)
        e = e * mask[None, :, :]
        att = jax.nn.softmax(e, axis=2)
        h_prime = jnp.einsum('bij,bjf->bif', att, h)
        return jax.nn.elu(h_prime + beta * h)
    h = jnp.maximum(_layernorm(x, axis=-1), 0.0)
    x = x + _L0_gnn_ref(h, adj, L0_gnn_weight, L0_gnn_bias)
    h = jnp.maximum(_layernorm(x, axis=-1), 0.0)
    x = x + _L1_gnn_ref(h, L1_gnn_W, L1_gnn_a, L1_gnn_beta, adj)
    return x

_drawn_inputs = setup_inputs


def setup_inputs(seed=0):
    import zlib

    import numpy as np

    out = dict(_drawn_inputs(seed))
    spreads = {'L0_gnn_bias': (0.0, 0.1)}
    factors = {'L1_gnn_a': 8.0}
    for name, (base, spread) in spreads.items():
        noise = np.random.default_rng([zlib.crc32(name.encode()), seed]).standard_normal(out[name].shape)
        drawn = base * np.exp(spread * noise) if base else spread * noise
        out[name] = jnp.asarray(drawn.astype(out[name].dtype))
    for name, factor in factors.items():
        out[name] = (out[name] * factor).astype(out[name].dtype)
    return out
```

```python
from contextlib import ExitStack

import concourse.bass as bass
from concourse import mybir

ALU = mybir.AluOpType
ACT = mybir.ActivationFunctionType
AX = mybir.AxisListType
F32 = mybir.dt.float32
F16 = mybir.dt.float16

P = 128
B, N, C = 8, 1024, 256
NT = N // P
CT = C // P
HALF = 512
NK = N // HALF
TK = HALF // P
GROUPS = NK * CT
EPS = 1e-5
SLOPE = 0.2
ADJ_SCALE = 8.0
W_SCALE = 16.0
LOWEST = -3.0e38
RING = 4
ELU_RING = 2
ADJ_CUTS = 4
CUT = N // ADJ_CUTS
PAIRS = 3


def two_layers(nc, x, adj, w0, bias, w1, a, beta, out):
    with ExitStack() as ctx:
        def sb(name, shape, dt):
            return ctx.enter_context(nc.sbuf_tensor(name, shape, dt))

        def sem(name):
            return ctx.enter_context(nc.semaphore(name))

        adj_rows = sb("adj_rows", [P, NT, N], F32)
        adjT_hi = sb("adjT_hi", [P, NT, N], F16)
        adjT_lo = sb("adjT_lo", [P, NT, N], F16)
        xin = sb("xin", [P, 2, NT, C], F32)
        xmid = sb("xmid", [P, 2, NT, C], F32)
        h_f32 = sb("h_f32", [P, NT, C], F32)
        h1_hi = sb("h1_hi", [P, NT, C], F16)
        h1_lo = sb("h1_lo", [P, NT, C], F16)
        h2_hi = sb("h2_hi", [P, 2, NT, C], F16)
        h2_lo = sb("h2_lo", [P, 2, NT, C], F16)
        u_hi = sb("u_hi", [P, CT, HALF], F16)
        u_lo = sb("u_lo", [P, CT, HALF], F16)    
        v_hi = sb("v_hi", [P, CT, HALF], F16)
        v_lo = sb("v_lo", [P, CT, HALF], F16)    
        pT_hi = sb("pT_hi", [P, NK, NT, HALF], F16)
        pT_lo = sb("pT_lo", [P, NK, NT, HALF], F16)
        score = sb("score", [P, RING, N], F32)
        s2_rows = sb("s2_rows", [P, N], F32)
        elu_neg = sb("elu_neg", [P, ELU_RING, C], F32)
        elu_pos = sb("elu_pos", [P, ELU_RING, C], F32)
        ident = sb("ident", [P, P], F32)
        ones = sb("ones", [P, P], F32)
        bias_rows = sb("bias_rows", [P, C], F32)
        w0_hi = sb("w0_hi", [P, CT, C], F16)
        w0_lo = sb("w0_lo", [P, CT, C], F16)
        w1_hi = sb("w1_hi", [P, CT, C], F16)
        w1_lo = sb("w1_lo", [P, CT, C], F16)
        wa_rows = sb("wa_rows", [P, 2, C], F32)
        beta_col = sb("beta_col", [P, 1], F32)
        a_cols = sb("a_cols", [P, 2 * CT], F32)
        neg_half = sb("neg_half", [P, NT], F32)
        deg = sb("deg", [P, NT], F32)
        deg_pos = sb("deg_pos", [P, NT], F32)
        dinv = sb("dinv", [P, NT], F32)
        dinv_out = sb("dinv_out", [P, NT], F32)
        st1 = sb("st1", [P, NT, 6], F32)
        mv1 = sb("mv1", [P, NT, 2], F32)
        ve1 = sb("ve1", [P, NT], F32)
        rs1 = sb("rs1", [P, NT], F32)
        sc1 = sb("sc1", [P, NT], F32)
        mr1 = sb("mr1", [P, NT], F32)
        sh1 = sb("sh1", [P, NT], F32)
        st2 = sb("st2", [P, NT, 6], F32)
        mv2 = sb("mv2", [P, NT, 2], F32)
        ve2 = sb("ve2", [P, NT], F32)
        sc2 = sb("sc2", [P, NT], F32)
        mr2 = sb("mr2", [P, NT], F32)
        sh2 = sb("sh2", [P, NT], F32)
        s1_col = sb("s1_col", [P, 2, NT], F32)
        s1_col4 = sb("s1_col4", [P, 2, NT], F32)
        s2_col = sb("s2_col", [P, NT], F32)
        dots_out = sb("dots_out", [P, C], F32)
        max5 = sb("max5", [P, NT], F32)
        neg_max = sb("neg_max", [P, NT], F32)
        row_sum = sb("row_sum", [P, 2, NT], F32)
        beta_sum = sb("beta_sum", [P, NT], F32)
        sum_scaled = sb("sum_scaled", [P, NT], F32)
        inv_sum = sb("inv_sum", [P, 2, NT], F32)
        w0_raw = score[:, 0, 0:CT * C].rearrange("p (k c) -> p k c", k=CT)
        w1_raw = score[:, 0, CT * C:2 * CT * C].rearrange("p (k c) -> p k c", k=CT)
        w1T = score[:, 1, 0:CT * C].rearrange("p (k c) -> p k c", k=CT)
        a_wide = score[:, 1, CT * C:CT * C + 4 * P].rearrange("p (k c) -> p k c", k=2 * CT)

        mix_ps = ctx.enter_context(nc.psum_tensor("mix_ps", [P, 2, HALF], F32))
        proj_ps = ctx.enter_context(nc.psum_tensor("proj_ps", [P, TK, C], F32))
        tr_ps = ctx.enter_context(nc.psum_tensor("tr_ps", [P, 2, N], F32))

        small_loaded = sem("small_loaded")
        adj_loaded = [sem(f"adj_loaded_{cut}") for cut in range(ADJ_CUTS)]
        x_loaded = [sem(f"x_loaded_{parity}") for parity in range(2)]
        out_stored = [[sem(f"out_stored_{parity}_{k}") for k in range(NK)] for parity in range(2)]
        consts = sem("consts")
        wide_made, wT_tr, wT_made, wa_done, wa_made = map(sem, ("wide_made", "wT_tr", "wT_made", "wa_done", "wa_made"))
        w_split, w_scaled, deg_made, dinv_made = map(sem, ("w_split", "w_scaled", "deg_made", "dinv_made"))
        adjT_tr, adjT_hi_made, adjT_lo_made = map(sem, ("adjT_tr", "adjT_hi_made", "adjT_lo_made"))
        bn1, stats1, norm1_step, norm1, h1_made, h1_hi_made, h1_split, biased = map(
            sem, ("bn1", "stats1", "norm1_step", "norm1", "h1_made", "h1_hi_made", "h1_split", "biased"))
        u_done, u_hi_made, u_split, p0_done, x1_made = map(sem, ("u_done", "u_hi_made", "u_split", "p0_done", "x1_made"))
        bn2, stats2, norm2_step, norm2, h2_made, h2_hi_made, h2_split = map(
            sem, ("bn2", "stats2", "norm2_step", "norm2", "h2_made", "h2_hi_made", "h2_split"))
        dots, dots4, s2_diag, s2_done, s2_made = map(sem, ("dots", "dots4", "s2_diag", "s2_done", "s2_made"))
        relu_made, leaky, masked, neg_max_made, exp_made, beta_made, p_made = map(
            sem, ("relu_made", "leaky", "masked", "neg_max_made", "exp_made", "beta_made", "p_made"))
        p_tr, pT_hi_made, pT_split = map(sem, ("p_tr", "pT_hi_made", "pT_split"))
        v_done, v_hi_made, v_split, p1_done = map(sem, ("v_done", "v_hi_made", "v_split", "p1_done"))
        scaled, inv_made = map(sem, ("scaled", "inv_made"))
        elu_exp, elu_relu, elu_low, elu_sum, out_made = map(sem, ("elu_exp", "elu_relu", "elu_low", "elu_sum", "out_made"))

        adj_cols = adj.rearrange("(t p) m -> p t m", p=P)
        x_rows = x.rearrange("b (t p) c -> b p t c", p=P)
        out_rows = out.rearrange("b (t p) c -> b p t c", p=P)

        def wait(eng, semaphore, value):
            if not isinstance(value, int) or value > 0:
                eng.wait_ge(semaphore, value)

        passed = sem("passed")

        def wait_first(eng, semaphore, value):
            if not isinstance(value, int):
                eng.wait_ge(semaphore, value)
                eng.sem_inc(passed, 1)
            elif value > 0:
                eng.wait_ge(semaphore, value)

        def bank_end(t):
            return t // 2 * 2 + 2

        def of(rows, batch):
            if isinstance(batch, int):
                return rows[batch]
            return rows[bass.ds(batch, 1)].rearrange("o p t c -> p (o t) c")

        def iterations(eng, run):
            run(-1, -1, 0)
            run(0, 0, 0)
            with eng.Fori(0, PAIRS) as q:
                run(q * 2 + 1, 1, q)
                run(q * 2 + 2, 2, q)
            run(B - 1, B - 1, 0)
            run(B, B, 0)

        def has_prev(s): return s >= 1
        def has_attn(s): return 0 <= s < B
        def has_next(s): return s < B - 1

        block = ctx.enter_context(nc.Block())

        @block.sync
        def _(sp):
            for cut in range(ADJ_CUTS):
                sp.dma_start(adj_rows[:, :, cut * CUT:(cut + 1) * CUT],
                             adj_cols[:, :, cut * CUT:(cut + 1) * CUT]).then_inc(adj_loaded[cut], 16)

            def load(b, s):
                wait(sp, x1_made, NT * (b - 1))
                sp.dma_start(xin[:, s % 2], of(x_rows, b)).then_inc(x_loaded[s % 2], 16)

            def store(b, s):
                for k in range(NK):
                    sp.wait_ge(out_made, ELU_RING + NT * b + TK * (k + 1))
                    sp.dma_start(of(out_rows, b)[:, k * TK:(k + 1) * TK],
                                 xmid[:, s % 2, k * TK:(k + 1) * TK]).then_inc(out_stored[s % 2][k], 16)

            load(0, 0)
            load(1, 1)
            load(2, 2)
            with sp.Fori(0, 2) as q:
                for c in range(2):
                    load(q * 2 + c + 3, c + 3)
                    store(q * 2 + c, c)
            load(7, 7)
            for b in range(4, B):
                store(b, b)
            for parity in range(2):
                for k in range(NK):
                    sp.wait_ge(out_stored[parity][k], 16 * (B // 2))

        @block.gpsimd
        def _(pool):
            pool.memset(elu_neg[:], 0.0).then_inc(out_made, ELU_RING)
            pool.memset(ident[:], 0.0).then_inc(consts, 1)
            pool.memset(ones[:], 1.0).then_inc(consts, 1)
            pool.memset(neg_half[:], -0.5).then_inc(consts, 1)
            pool.wait_ge(consts, 3)
            pool.affine_select(out=ident[:], in_=ident[:], compare_op=ALU.not_equal, fill=1.0, base=0,
                               pattern=[[-1, P]], channel_multiplier=1).then_inc(consts, 1)
            pool.wait_ge(deg_made, NT)
            pool.tensor_scalar(deg_pos[:], deg[:], 0.0, None, ALU.is_gt).then_inc(dinv_made, 1)
            pool.tensor_scalar(dinv_out[:], deg[:], 1.2e-38, None, ALU.max).then_inc(dinv_made, 1)
            pool.wait_ge(dinv_made, 2)
            pool.tensor_tensor(dinv[:], dinv_out[:], neg_half[:], ALU.pow).then_inc(dinv_made, 1)
            pool.wait_ge(dinv_made, 3)
            pool.tensor_tensor(dinv[:], dinv[:], deg_pos[:], ALU.mult).then_inc(dinv_made, 1)
            pool.wait_ge(dinv_made, 4)
            pool.tensor_scalar(dinv_out[:], dinv[:], 1.0 / (ADJ_SCALE * W_SCALE), None, ALU.mult).then_inc(dinv_made, 1)

            def norm_1(bb, k):
                t = slice(k * TK, (k + 1) * TK)
                n = 4 * (NK * bb + k)
                wait_first(pool, stats1, NT * bb + TK * (k + 1))
                pool.tensor_scalar(ve1[:, t], mv1[:, t, 1], EPS, None, ALU.add).then_inc(norm1_step, 1)
                pool.wait_ge(norm1_step, n + 1)
                pool.tensor_tensor(rs1[:, t], ve1[:, t], neg_half[:, t], ALU.pow).then_inc(norm1_step, 1)
                pool.wait_ge(norm1_step, n + 2)
                pool.tensor_tensor(sc1[:, t], rs1[:, t], dinv[:, t], ALU.mult).then_inc(norm1_step, 1)
                pool.wait_ge(norm1_step, n + 3)
                pool.tensor_tensor(mr1[:, t], mv1[:, t, 0], sc1[:, t], ALU.mult).then_inc(norm1_step, 1)
                wait_first(pool, norm1_step, n + 4)
                pool.tensor_scalar(sh1[:, t], mr1[:, t], -1.0, None, ALU.mult).then_inc(norm1, 1)

            def norm_2(bb, k):
                t = slice(k * TK, (k + 1) * TK)
                n = 3 * (NK * bb + k)
                wait_first(pool, stats2, NT * bb + TK * (k + 1))
                pool.tensor_scalar(ve2[:, t], mv2[:, t, 1], EPS, None, ALU.add).then_inc(norm2_step, 1)
                pool.wait_ge(norm2_step, n + 1)
                pool.tensor_tensor(sc2[:, t], ve2[:, t], neg_half[:, t], ALU.pow).then_inc(norm2_step, 1)
                pool.wait_ge(norm2_step, n + 2)
                pool.tensor_tensor(mr2[:, t], mv2[:, t, 0], sc2[:, t], ALU.mult).then_inc(norm2_step, 1)
                wait_first(pool, norm2_step, n + 3)
                pool.tensor_scalar(sh2[:, t], mr2[:, t], -1.0, None, ALU.mult).then_inc(norm2, 1)

            def split_1(bb, k):
                for t in range(k * TK, (k + 1) * TK):
                    if t == 0:
                        wait(pool, u_done, GROUPS * bb)
                    wait_first(pool, h1_made, NT * bb + t + 1)
                    pool.tensor_copy(h1_hi[:, t], h_f32[:, t]).then_inc(h1_hi_made, 1)
                    pool.wait_ge(h1_hi_made, NT * bb + t + 1)
                    pool.tensor_tensor(h1_lo[:, t], h_f32[:, t], h1_hi[:, t], ALU.subtract).then_inc(h1_split, 1)

            def split_2(bb, s, k):
                for t in range(k * TK, (k + 1) * TK):
                    if t == 0:
                        wait(pool, v_done, GROUPS * (bb - 1))
                    wait_first(pool, h2_made, NT * bb + t + 1)
                    pool.tensor_copy(h2_hi[:, s % 2, t], h_f32[:, t]).then_inc(h2_hi_made, 1)
                    pool.wait_ge(h2_hi_made, NT * bb + t + 1)
                    pool.tensor_tensor(h2_lo[:, s % 2, t], h_f32[:, t], h2_hi[:, s % 2, t], ALU.subtract).then_inc(h2_split, 1)

            def add_bias(bb, s):
                for t in range(NT):
                    pool.wait_ge(h1_made, NT * bb + t + 1)
                    pool.tensor_tensor(xin[:, s % 2, t], xin[:, s % 2, t], bias_rows[:], ALU.add).then_inc(biased, 1)

            def output(bb, s, k):
                for t in range(k * TK, (k + 1) * TK):
                    pool.wait_ge(elu_low, NT * bb + t + 1)
                    pool.tensor_tensor(xmid[:, s % 2, t], xmid[:, s % 2, t], elu_neg[:, t % ELU_RING], ALU.add).then_inc(elu_sum, 1)
                    pool.wait_ge(elu_sum, NT * bb + t + 1)
                    pool.tensor_tensor(xmid[:, s % 2, t], xmid[:, s % 2, t], elu_pos[:, t % ELU_RING], ALU.add).then_inc(out_made, 1)

            def run(b, s, q):
                if has_next(s):
                    norm_1(b + 1, 0)
                    norm_1(b + 1, 1)
                if has_prev(s):
                    output(b - 1, s - 1, 0)
                if has_next(s):
                    split_1(b + 1, 0)
                    split_1(b + 1, 1)
                    add_bias(b + 1, s + 1)
                if has_prev(s):
                    output(b - 1, s - 1, 1)
                if has_next(s):
                    norm_2(b + 1, 0)
                    split_2(b + 1, s + 1, 0)
                    norm_2(b + 1, 1)
                    split_2(b + 1, s + 1, 1)

            pool.wait_ge(dinv_made, 5)
            pool.wait_ge(small_loaded, 16 * 5)
            iterations(pool, run)

        @block.scalar
        def _(act):
            act.dma_start(w0_raw, w0.rearrange("(k p) c -> p k c", p=P)).then_inc(small_loaded, 16)
            act.dma_start(w1_raw, w1.rearrange("(k p) c -> p k c", p=P)).then_inc(small_loaded, 16)
            act.dma_start(a_cols[:], a.rearrange("(k p) o -> p (k o)", p=P), allow_slow_non_contiguous=True).then_inc(small_loaded, 16)
            act.dma_start(bias_rows[:], bias.rearrange("(o c) -> o c", o=1).broadcast_to([P, C])).then_inc(small_loaded, 16)
            act.dma_start(beta_col[:], beta.rearrange("(o c) -> o c", o=1).broadcast_to([P, 1])).then_inc(small_loaded, 16)
            act.wait_ge(small_loaded, 16 * 5)
            act.activation(w0_hi[:], w0_raw, ACT.Copy, scale=W_SCALE).then_inc(w_scaled, 1)
            act.activation(w1_hi[:], w1_raw, ACT.Copy, scale=W_SCALE).then_inc(w_scaled, 1)
            for m in range(NT):
                act.wait_ge(adjT_tr, m + 1)
                act.activation(adjT_hi[:, m], tr_ps[:, m % 2], ACT.Copy, scale=ADJ_SCALE).then_inc(adjT_hi_made, 1)

            def norm_relu_1(bb, s, k):
                act.wait_ge(norm1, NK * bb + k + 1)
                for t in range(k * TK, (k + 1) * TK):
                    act.activation(h_f32[:, t], xin[:, s % 2, t], ACT.Relu, bias=sh1[:, t:t + 1],
                                   scale=sc1[:, t:t + 1]).then_inc(h1_made, 1)

            def norm_relu_2(bb, s, k):
                act.wait_ge(norm2, NK * bb + k + 1)
                for t in range(k * TK, (k + 1) * TK):
                    act.wait_ge(h1_split, NT * bb + t + 1)
                    act.activation(h_f32[:, t], xmid[:, s % 2, t], ACT.Relu, bias=sh2[:, t:t + 1],
                                   scale=sc2[:, t:t + 1]).then_inc(h2_made, 1)

            def keep_s2(b, s):
                wait(act, leaky, NT * b)
                act.wait_ge(s2_done, b + 1)
                act.activation(s2_rows[:], tr_ps[:, s % 2], ACT.Copy).then_inc(s2_made, 1)

            def relu(b, s, t):
                if t == 0:
                    act.wait_ge(dots4, NK * b + NK)
                    act.wait_ge(s2_made, b + 1)
                wait(act, p_tr, NT * b + t + 1 - RING)
                act.activation(score[:, t % RING], s2_rows[:], ACT.Relu, bias=s1_col4[:, s % 2, t:t + 1],
                               scale=4.0).then_inc(relu_made, 1)

            def exp(b, s, t):
                act.wait_ge(neg_max_made, NT * b + t + 1)
                act.activation(score[:, t % RING], score[:, t % RING], ACT.Exp, bias=neg_max[:, t:t + 1],
                               scale=SLOPE, accum_out=row_sum[:, s % 2, t:t + 1]).then_inc(exp_made, 1)

            def hi_pT(b, s, t):
                k = t // TK
                if t % TK == 0:
                    wait(act, v_done, GROUPS * (b - 1) + CT * (k + 1))
                act.wait_ge(p_tr, NT * b + t + 1)
                act.activation(pT_hi[:, k, :, (t % TK) * P:(t % TK + 1) * P],
                               tr_ps[:, (s + t + 1) % 2].rearrange("p (j i) -> p j i", j=NT),
                               ACT.Copy).then_inc(pT_hi_made, 1)

            def hi_u(bb, g):
                wait(act, p0_done, NT * bb + TK * (g // CT))
                act.wait_ge(u_done, GROUPS * bb + g + 1)
                act.activation(u_hi[:, g % CT], mix_ps[:, g % 2], ACT.Copy).then_inc(u_hi_made, 1)

            def hi_v(bb, g):
                wait(act, p1_done, NT * bb + TK * (g // CT))
                act.wait_ge(v_done, GROUPS * bb + g + 1)
                act.activation(v_hi[:, g % CT], mix_ps[:, g % 2], ACT.Copy).then_inc(v_hi_made, 1)

            def elu(bb, s, k):
                act.wait_ge(inv_made, NK * bb + k + 1)
                for t in range(k * TK, (k + 1) * TK):
                    act.wait_ge(out_made, ELU_RING + NT * bb + t + 1 - ELU_RING)
                    act.wait_ge(p1_done, NT * bb + bank_end(t))
                    inv = inv_sum[:, s % 2, t:t + 1]
                    act.activation(elu_neg[:, t % ELU_RING], proj_ps[:, t % TK], ACT.Exp, scale=inv).then_inc(elu_exp, 1)
                    act.activation(elu_pos[:, t % ELU_RING], proj_ps[:, t % TK], ACT.Relu, scale=inv).then_inc(elu_relu, 1)

            def run(b, s, q):
                if has_prev(s):
                    elu(b - 1, s - 1, 0)
                if has_attn(s):
                    keep_s2(b, s)
                    relu(b, s, 0)
                    relu(b, s, 1)
                if has_next(s):
                    norm_relu_1(b + 1, s + 1, 0)
                for t in range(NT):
                    if has_attn(s):
                        exp(b, s, t)
                        if t + 2 < NT:
                            relu(b, s, t + 2)
                        if t >= 1:
                            hi_pT(b, s, t - 1)
                    if t == 0 and has_next(s):
                        norm_relu_1(b + 1, s + 1, 1)
                    if t in (0, 1) and has_prev(s):
                        hi_v(b - 1, 2 + t)
                    if t == 3 and has_prev(s):
                        elu(b - 1, s - 1, 1)
                    if t == 5 and has_next(s):
                        norm_relu_2(b + 1, s + 1, 0)
                    if t in (2, 3, 4, 5) and has_next(s):
                        hi_u(b + 1, t - 2)
                    if t in (6, 7) and has_attn(s):
                        hi_v(b, t - 6)
                if has_attn(s):
                    hi_pT(b, s, NT - 1)
                if has_next(s):
                    norm_relu_2(b + 1, s + 1, 1)

            act.wait_ge(dinv_made, 5)
            iterations(act, run)

        @block.tensor
        def _(pe):
            def product(dst, left, right, first, last):
                pe.matmul(dst, left[0], right[0], start=first, stop=False)
                pe.matmul(dst, left[0], right[1], start=False, stop=False)
                return pe.matmul(dst, left[1], right[0], start=False, stop=last)

            pe.wait_ge(consts, 4)
            pe.wait_ge(small_loaded, 16 * 5)
            for k in range(CT):
                for f in range(CT):
                    mm = pe.transpose(proj_ps[:, f, k * P:(k + 1) * P], w1_raw[:, k, f * P:(f + 1) * P], ident[:])
            mm.then_inc(wT_tr, 1)
            pe.wait_ge(wT_made, 1)
            pe.wait_ge(wide_made, 4)
            for i in range(2):
                for f in range(CT):
                    mm = pe.matmul(proj_ps[:, 2 + i], a_wide[:, i * CT + f], w1T[:, f], start=f == 0, stop=f == CT - 1)
            mm.then_inc(wa_done, 1)
            for m in range(NT):
                pe.wait_ge(adj_loaded[m * P // CUT], 16)
                if m >= 2:
                    pe.wait_ge(adjT_lo_made, m - 1)
                for n in range(NT):
                    mm = pe.transpose(tr_ps[:, m % 2, n * P:(n + 1) * P], adj_rows[:, n, m * P:(m + 1) * P], ident[:])
                mm.then_inc(adjT_tr, 1)

            def mix_u(bb, g):
                k, c = g // CT, g % CT
                cols = slice(c * P, (c + 1) * P)
                rows = slice(k * HALF, (k + 1) * HALF)
                for m in range(NT):
                    if g == 0:
                        pe.wait_ge(h1_split, NT * bb + m + 1)
                    mm = product(mix_ps[:, g % 2], (h1_hi[:, m, cols], h1_lo[:, m, cols]),
                                 (adjT_hi[:, m, rows], adjT_lo[:, m, rows]), m == 0, m == NT - 1)
                mm.then_inc(u_done, 1)

            def mix_v(bb, s, g):
                k, c = g // CT, g % CT
                cols = slice(c * P, (c + 1) * P)
                pe.wait_ge(pT_split, NT * bb + TK * (k + 1))
                for m in range(NT):
                    if g == 0:
                        pe.wait_ge(h2_split, NT * bb + m + 1)
                    mm = product(mix_ps[:, g % 2], (h2_hi[:, s % 2, m, cols], h2_lo[:, s % 2, m, cols]),
                                 (pT_hi[:, k, m], pT_lo[:, k, m]), m == 0, m == NT - 1)
                mm.then_inc(v_done, 1)

            def project(left_hi, left_lo, w_hi, w_lo, i, done):
                rows = slice(i * P, (i + 1) * P)
                for c in range(CT):
                    mm = product(proj_ps[:, i], (left_hi[:, c, rows], left_lo[:, c, rows]),
                                 (w_hi[:, c], w_lo[:, c]), c == 0, c == CT - 1)
                mm.then_inc(done, 1)

            def project_u(bb, s, k):
                pe.wait_ge(u_split, GROUPS * bb + CT * (k + 1))
                for i in range(TK):
                    if k == 1:
                        pe.wait_ge(x1_made, NT * bb + bank_end(i))
                    elif s >= 2:
                        pe.wait_ge(elu_relu, NT * (bb - 2) + TK + bank_end(i))
                    else:
                        wait(pe, x1_made, NT * (bb - 1) + TK + bank_end(i))
                    project(u_hi, u_lo, w0_hi, w0_lo, i, p0_done)

            def project_v(bb, s, k):
                pe.wait_ge(v_split, GROUPS * bb + CT * (k + 1))
                for i in range(TK):
                    if k == 1:
                        pe.wait_ge(elu_relu, NT * bb + bank_end(i))
                    elif s < B - 1:
                        pe.wait_ge(x1_made, NT * (bb + 1) + TK + bank_end(i))
                    else:
                        pe.wait_ge(elu_relu, NT * (bb - 1) + TK + bank_end(i))
                    project(v_hi, v_lo, w1_hi, w1_lo, i, p1_done)

            def spread_s2(b, s):
                wait(pe, pT_split, NT * b - 1)
                for t in range(NT):
                    pe.wait_ge(s2_diag, NT * b + t + 1)
                    mm = pe.matmul(tr_ps[:, s % 2, t * P:(t + 1) * P], ones[:], h_f32[:, t, 0:P], start=True, stop=True)
                mm.then_inc(s2_done, 1)

            def transpose_p(b, s, t):
                if t == 1:
                    pe.wait_ge(s2_made, b + 1)
                else:
                    wait(pe, pT_split, NT * b + t - 1 if t else NT * b)
                pe.wait_ge(p_made, NT * b + t + 1)
                for j in range(NT):
                    mm = pe.transpose(tr_ps[:, (s + t + 1) % 2, j * P:(j + 1) * P],
                                      score[:, t % RING, j * P:(j + 1) * P], ident[:])
                mm.then_inc(p_tr, 1)

            def run(b, s, q):
                if has_prev(s):
                    project_v(b - 1, s - 1, 0)
                if has_attn(s):
                    spread_s2(b, s)
                for t in range(NT):
                    if t in (0, 1) and has_prev(s):
                        pe.wait_ge(v_split, GROUPS * (b - 1) + t + 1)
                        mix_v(b - 1, s - 1, 2 + t)
                    if t in (2, 3) and has_next(s):
                        if has_prev(s):
                            pe.wait_ge(v_split, GROUPS * (b - 1) + t + 1)
                        else:
                            wait(pe, u_split, GROUPS * b + t + 1)
                        mix_u(b + 1, t - 2)
                    if t in (4, 5) and has_next(s):
                        pe.wait_ge(u_split, GROUPS * (b + 1) + t - 3)
                        mix_u(b + 1, t - 2)
                    if t in (6, 7) and has_attn(s):
                        if has_next(s):
                            pe.wait_ge(u_split, GROUPS * (b + 1) + t - 3)
                        else:
                            pe.wait_ge(v_split, GROUPS * (b - 1) + t - 3)
                        mix_v(b, s, t - 6)
                    if t == 2 and has_prev(s):
                        project_v(b - 1, s - 1, 1)
                    if t == 4 and has_next(s):
                        project_u(b + 1, s + 1, 0)
                    if t == 6 and has_next(s):
                        project_u(b + 1, s + 1, 1)
                    if has_attn(s):
                        transpose_p(b, s, t)

            pe.wait_ge(adjT_lo_made, NT)
            pe.wait_ge(w_split, 2)
            pe.wait_ge(wa_made, 1)
            iterations(pe, run)

        @block.vector
        def _(dve):
            dve.wait_ge(small_loaded, 16 * 5)
            dve.wait_ge(consts, 4)
            for i in range(2 * CT):
                dve.tensor_scalar(a_wide[:, i], ones[:], a_cols[:, i:i + 1], None, ALU.mult).then_inc(wide_made, 1)
            dve.wait_ge(wT_tr, 1)
            dve.tensor_copy(w1T, proj_ps[:, 0:CT]).then_inc(wT_made, 1)
            dve.wait_ge(w_scaled, 2)
            dve.scalar_tensor_tensor(w0_lo[:], w0_raw, W_SCALE, w0_hi[:], ALU.mult, ALU.subtract).then_inc(w_split, 1)
            dve.scalar_tensor_tensor(w1_lo[:], w1_raw, W_SCALE, w1_hi[:], ALU.mult, ALU.subtract).then_inc(w_split, 1)
            dve.wait_ge(wa_done, 1)
            dve.tensor_copy(wa_rows[:], proj_ps[:, 2:4]).then_inc(wa_made, 1)
            for m in range(NT):
                dve.wait_ge(adjT_hi_made, m + 1)
                dve.scalar_tensor_tensor(adjT_lo[:, m], tr_ps[:, m % 2], ADJ_SCALE, adjT_hi[:, m], ALU.mult,
                                         ALU.subtract).then_inc(adjT_lo_made, 1)
            for cut in range(ADJ_CUTS):
                dve.wait_ge(adj_loaded[cut], 16)
            for t in range(NT):
                dve.reduce_sum(deg[:, t:t + 1], adj_rows[:, t], AX.X).then_inc(deg_made, 1)

            def stats_1(bb, s, q):
                dve.wait_ge(x_loaded[s % 2], (q + s // 2) * 16 + 16)
                for t in range(NT):
                    dve.bn_stats(st1[:, t], xin[:, s % 2, t]).then_inc(bn1, 1)
                for t in range(NT):
                    wait_first(dve, bn1, NT * bb + t + 1)
                    dve.bn_aggr(mv1[:, t], st1[:, t]).then_inc(stats1, 1)

            def x1_stats_2(bb, s, q, k):
                tiles = range(k * TK, (k + 1) * TK)
                wait(dve, out_stored[s % 2][k], (q + s // 2) * 16)
                for t in tiles:
                    dve.wait_ge(biased, NT * bb + t + 1)
                    dve.wait_ge(p0_done, NT * bb + bank_end(t))
                    dve.scalar_tensor_tensor(xmid[:, s % 2, t], proj_ps[:, t % TK], dinv_out[:, t:t + 1],
                                             xin[:, s % 2, t], ALU.mult, ALU.add).then_inc(x1_made, 1)
                for t in tiles:
                    dve.wait_ge(x1_made, NT * bb + t + 1)
                    dve.bn_stats(st2[:, t], xmid[:, s % 2, t]).then_inc(bn2, 1)
                for t in tiles:
                    wait_first(dve, bn2, NT * bb + t + 1)
                    dve.bn_aggr(mv2[:, t], st2[:, t]).then_inc(stats2, 1)

            def dots_2(bb, s, k):
                tiles = range(k * TK, (k + 1) * TK)
                for t in tiles:
                    wait(dve, dots, 2 * (NT * bb + t) - 1)
                    dve.wait_ge(h2_made, NT * bb + t + 1)
                    dve.tensor_tensor_reduce(dots_out[:], h_f32[:, t], wa_rows[:, 0], 1.0, 0.0, ALU.mult,
                                             ALU.add, s1_col[:, s % 2, t:t + 1]).then_inc(dots, 1)
                    dve.wait_ge(h2_split, NT * bb + t + 1)
                    dve.tensor_tensor_reduce(h_f32[:, t], h_f32[:, t], wa_rows[:, 1], 1.0, 0.0, ALU.mult,
                                             ALU.add, s2_col[:, t:t + 1]).then_inc(dots, 1)
                for t in tiles:
                    dve.wait_ge(dots, 2 * (NT * bb + t + 1))
                    dve.tensor_scalar(h_f32[:, t, 0:P], ident[:], s2_col[:, t:t + 1], None, ALU.mult).then_inc(s2_diag, 1)
                dve.tensor_scalar(s1_col4[:, s % 2, k * TK:(k + 1) * TK], s1_col[:, s % 2, k * TK:(k + 1) * TK],
                                  4.0, None, ALU.mult).then_inc(dots4, 1)

            def score_max(b, s, t):
                dve.wait_ge(relu_made, NT * b + t + 1)
                dve.scalar_tensor_tensor(score[:, t % RING], s2_rows[:], s1_col[:, s % 2, t:t + 1], score[:, t % RING],
                                         ALU.add, ALU.add).then_inc(leaky, 1)
                wait_first(dve, leaky, NT * b + t + 1)
                dve.tensor_tensor_reduce(score[:, t % RING], score[:, t % RING], adj_rows[:, t], 1.0, LOWEST, ALU.mult,
                                         ALU.max, max5[:, t:t + 1]).then_inc(masked, 1)
                dve.wait_ge(masked, NT * b + t + 1)
                dve.tensor_scalar(neg_max[:, t:t + 1], max5[:, t:t + 1], -SLOPE, None, ALU.mult).then_inc(neg_max_made, 1)

            def add_beta(b, s, t):
                dve.wait_ge(exp_made, NT * b + t + 1)
                dve.tensor_scalar(beta_sum[:, t:t + 1], row_sum[:, s % 2, t:t + 1], beta_col[:, 0:1], None,
                                  ALU.mult).then_inc(beta_made, 1)
                dve.wait_ge(beta_made, NT * b + t + 1)
                diag = score[:, t % RING, t * P:(t + 1) * P]
                dve.scalar_tensor_tensor(diag, ident[:], beta_sum[:, t:t + 1], diag, ALU.mult, ALU.add).then_inc(p_made, 1)

            def invert_sums(b, s, k):
                t = slice(k * TK, (k + 1) * TK)
                dve.tensor_scalar(sum_scaled[:, t], row_sum[:, s % 2, t], W_SCALE, None, ALU.mult).then_inc(scaled, 1)
                dve.wait_ge(scaled, NK * b + k + 1)
                dve.reciprocal(inv_sum[:, s % 2, t], sum_scaled[:, t]).then_inc(inv_made, 1)

            def lo_pT(b, s, t):
                k = t // TK
                cols = slice((t % TK) * P, (t % TK + 1) * P)
                dve.wait_ge(pT_hi_made, NT * b + t + 1)
                dve.scalar_tensor_tensor(pT_lo[:, k, :, cols], tr_ps[:, (s + t + 1) % 2].rearrange("p (j i) -> p j i", j=NT),
                                         1.0, pT_hi[:, k, :, cols], ALU.mult, ALU.subtract).then_inc(pT_split, 1)

            def lo_u(bb, g):
                dve.wait_ge(u_hi_made, GROUPS * bb + g + 1)
                dve.scalar_tensor_tensor(u_lo[:, g % CT], mix_ps[:, g % 2], 1.0, u_hi[:, g % CT],
                                         ALU.mult, ALU.subtract).then_inc(u_split, 1)

            def lo_v(bb, g):
                dve.wait_ge(v_hi_made, GROUPS * bb + g + 1)
                dve.scalar_tensor_tensor(v_lo[:, g % CT], mix_ps[:, g % 2], 1.0, v_hi[:, g % CT],
                                         ALU.mult, ALU.subtract).then_inc(v_split, 1)

            def elu_neg_part(bb, k):
                for t in range(k * TK, (k + 1) * TK):
                    dve.wait_ge(elu_relu, NT * bb + t + 1)
                    dve.tensor_scalar(elu_neg[:, t % ELU_RING], elu_neg[:, t % ELU_RING], 1.0, -1.0, ALU.min, ALU.add).then_inc(elu_low, 1)

            def run(b, s, q):
                if has_next(s):
                    stats_1(b + 1, s + 1, q)
                if has_prev(s):
                    elu_neg_part(b - 1, 0)
                if has_attn(s):
                    score_max(b, s, 0)
                for t in range(NT):
                    if has_attn(s):
                        if t + 1 < NT:
                            score_max(b, s, t + 1)
                        add_beta(b, s, t)
                        if t >= 1:
                            lo_pT(b, s, t - 1)
                        if t == 4:
                            invert_sums(b, s, 0)
                    if t in (0, 1) and has_prev(s):
                        lo_v(b - 1, 2 + t)
                    if t == 3 and has_prev(s):
                        elu_neg_part(b - 1, 1)
                    if t == 6 and has_next(s):
                        dots_2(b + 1, s + 1, 0)
                    if t in (2, 3, 4, 5) and has_next(s):
                        lo_u(b + 1, t - 2)
                    if t in (6, 7) and has_attn(s):
                        lo_v(b, t - 6)
                    if t == 4 and has_next(s):
                        x1_stats_2(b + 1, s + 1, q, 0)
                    if t == 6 and has_next(s):
                        x1_stats_2(b + 1, s + 1, q, 1)
                if has_attn(s):
                    invert_sums(b, s, 1)
                    lo_pT(b, s, NT - 1)
                if has_next(s):
                    dots_2(b + 1, s + 1, 1)

            dve.wait_ge(wa_made, 1)
            dve.wait_ge(dinv_made, 5)
            iterations(dve, run)


_INS = ["x", "adj", "L0_gnn_weight", "L0_gnn_bias", "L1_gnn_W", "L1_gnn_a", "L1_gnn_beta"]


def kernel(**inputs):
    import numpy as np
    import concourse.bacc as bacc
    from concourse.bass_utils import run_bass_kernel_spmd

    nc = bacc.Bacc("TRN2", target_bir_lowering=False, num_devices=1)
    arrays, args = {}, []
    for name in _INS:
        a = np.ascontiguousarray(inputs[name])
        arrays["in_" + name] = a
        args.append(nc.dram_tensor("in_" + name, a.shape, mybir.dt.from_np(a.dtype), kind="ExternalInput").ap())
    args.append(nc.dram_tensor("out_x", inputs["x"].shape, F32, kind="ExternalOutput").ap())
    two_layers(nc, *args)
    r = run_bass_kernel_spmd(nc, [arrays], core_ids=[0])
    return r.results[0]["out_x"]
```

```python
from contextlib import ExitStack

import concourse.bass as bass
from concourse import mybir

ALU = mybir.AluOpType
ACT = mybir.ActivationFunctionType
AX = mybir.AxisListType
F32 = mybir.dt.float32
F16 = mybir.dt.float16

P = 128
B, N, C = 8, 1024, 256
NT = N // P
CT = C // P
HALF = 512
NK = N // HALF
TK = HALF // P
GROUPS = NK * CT
EPS = 1e-5
SLOPE = 0.2
ADJ_SCALE = 8.0
W_SCALE = 16.0
LOWEST = -3.0e38
RING = 4
ELU_RING = 2
ADJ_CUTS = 4
CUT = NT // ADJ_CUTS
PAIRS = 3


def two_layers(nc, x, adj, w0, bias, w1, a, beta, out):
    with ExitStack() as ctx:
        def sb(name, shape, dt):
            return ctx.enter_context(nc.sbuf_tensor(name, shape, dt))

        def sem(name):
            return ctx.enter_context(nc.semaphore(name))

        adj_rows = sb("adj_rows", [P, NT, N], F32)
        adjT_hi = sb("adjT_hi", [P, NT, N], F16)
        adjT_lo = sb("adjT_lo", [P, NT, N], F16)
        xin = sb("xin", [P, 2, NT, C], F32)
        xmid = sb("xmid", [P, 2, NT, C], F32)
        h1_f32 = sb("h1_f32", [P, TK, C], F32)
        h2_f32 = sb("h2_f32", [P, NT, C], F32)
        h1_hi = sb("h1_hi", [P, NT, C], F16)
        h1_lo = sb("h1_lo", [P, NT, C], F16)
        h2_hi = sb("h2_hi", [P, 2, NT, C], F16)
        h2_lo = sb("h2_lo", [P, 2, NT, C], F16)
        u_hi = sb("u_hi", [P, CT, HALF], F16)
        u_lo = sb("u_lo", [P, CT, HALF], F16)
        v_hi = sb("v_hi", [P, CT, HALF], F16)
        v_lo = sb("v_lo", [P, CT, HALF], F16)
        pT_hi = sb("pT_hi", [P, NK, NT, HALF], F16)
        pT_lo = sb("pT_lo", [P, NK, NT, HALF], F16)
        score = sb("score", [P, RING, N], F32)
        s2_rows = sb("s2_rows", [P, N], F32)
        elu_neg = sb("elu_neg", [P, ELU_RING, C], F32)
        elu_pos = sb("elu_pos", [P, ELU_RING, C], F32)
        ident = sb("ident", [P, P], F32)
        beta_ident = sb("beta_ident", [P, P], F32)
        bias_rows = sb("bias_rows", [P, C], F32)
        w0_hi = sb("w0_hi", [P, CT, C], F16)
        w0_lo = sb("w0_lo", [P, CT, C], F16)
        w1_hi = sb("w1_hi", [P, CT, C], F16)
        w1_lo = sb("w1_lo", [P, CT, C], F16)
        wa_rows = sb("wa_rows", [P, 2, C], F32)
        beta_col = sb("beta_col", [P, 1], F32)
        a_cols = sb("a_cols", [P, 2 * CT], F32)
        neg_half = sb("neg_half", [P, NT], F32)
        deg = sb("deg", [P, NT], F32)
        deg_pos = sb("deg_pos", [P, NT], F32)
        dinv = sb("dinv", [P, NT], F32)
        dinv_out = sb("dinv_out", [P, NT], F32)
        st1 = sb("st1", [P, NT, 6], F32)
        mv1 = sb("mv1", [P, NT, 2], F32)
        ve1 = sb("ve1", [P, NT], F32)
        rs1 = sb("rs1", [P, NT], F32)
        sc1 = sb("sc1", [P, NT], F32)
        mr1 = sb("mr1", [P, NT], F32)
        sh1 = sb("sh1", [P, NT], F32)
        st2 = sb("st2", [P, NT, 6], F32)
        mv2 = sb("mv2", [P, NT, 2], F32)
        ve2 = sb("ve2", [P, NT], F32)
        sc2 = sb("sc2", [P, NT], F32)
        mr2 = sb("mr2", [P, NT], F32)
        sh2 = sb("sh2", [P, NT], F32)
        s1_col = sb("s1_col", [P, 2, NT], F32)
        s1_col4 = sb("s1_col4", [P, 2, NT], F32)
        s2_col = sb("s2_col", [P, NT], F32)
        dots_out = sb("dots_out", [P, 2, C], F32)
        max5 = sb("max5", [P, NT], F32)
        neg_max = sb("neg_max", [P, NT], F32)
        row_sum = sb("row_sum", [P, 2, NT], F32)
        sum_scaled = sb("sum_scaled", [P, NT], F32)
        inv_sum = sb("inv_sum", [P, 2, NT], F32)
        ones = s2_rows[:, 0:P]
        w0_raw = score[:, 0, 0:CT * C].rearrange("p (k c) -> p k c", k=CT)
        w1_raw = score[:, 0, CT * C:2 * CT * C].rearrange("p (k c) -> p k c", k=CT)
        w1T = score[:, 1, 0:CT * C].rearrange("p (k c) -> p k c", k=CT)
        a_wide = score[:, 1, CT * C:CT * C + 4 * P].rearrange("p (k c) -> p k c", k=2 * CT)

        mix_ps = ctx.enter_context(nc.psum_tensor("mix_ps", [P, 2, HALF], F32))
        proj_ps = ctx.enter_context(nc.psum_tensor("proj_ps", [P, TK, C], F32))
        tr_ps = ctx.enter_context(nc.psum_tensor("tr_ps", [P, 2, N], F32))

        small_loaded = sem("small_loaded")
        adj_loaded = [sem(f"adj_loaded_{cut}") for cut in range(ADJ_CUTS)]
        x_loaded = [sem(f"x_loaded_{parity}") for parity in range(2)]
        out_stored = [[sem(f"out_stored_{parity}_{k}") for k in range(NK)] for parity in range(2)]
        consts = sem("consts")
        wide_made, wT_tr, wT_made, wa_done, wa_made = map(sem, ("wide_made", "wT_tr", "wT_made", "wa_done", "wa_made"))
        w_split, w_scaled, deg_even, deg_odd, dinv_made = map(sem, ("w_split", "w_scaled", "deg_even", "deg_odd", "dinv_made"))
        adjT_tr, adjT_hi_made, adjT_lo_made = map(sem, ("adjT_tr", "adjT_hi_made", "adjT_lo_made"))
        bn1, stats1, ve1_made, rs1_made, sc1_made, mr1_made, norm1, h1_made, h1_hi_made, h1_split, biased = map(
            sem, ("bn1", "stats1", "ve1_made", "rs1_made", "sc1_made", "mr1_made", "norm1", "h1_made", "h1_hi_made", "h1_split", "biased"))
        u_done, u_hi_made, u_split, p0_done, x1_made = map(sem, ("u_done", "u_hi_made", "u_split", "p0_done", "x1_made"))
        bn2, stats2, norm2_step, norm2, h2_made, h2_hi_made, h2_split = map(
            sem, ("bn2", "stats2", "norm2_step", "norm2", "h2_made", "h2_hi_made", "h2_split"))
        dots, dots4, s2_done, s2_made = map(sem, ("dots", "dots4", "s2_done", "s2_made"))
        relu_made, leaky, masked, neg_max_made, exp_made, beta_ready, p_made = map(
            sem, ("relu_made", "leaky", "masked", "neg_max_made", "exp_made", "beta_ready", "p_made"))
        p_tr, pT_hi_made, pT_split = map(sem, ("p_tr", "pT_hi_made", "pT_split"))
        v_done, v_hi_made, v_split, p1_done = map(sem, ("v_done", "v_hi_made", "v_split", "p1_done"))
        scaled, inv_made = map(sem, ("scaled", "inv_made"))
        elu_exp, elu_relu, elu_sum, out_made = map(sem, ("elu_exp", "elu_relu", "elu_sum", "out_made"))

        adj_tiles = adj.rearrange("(t p) m -> p t m", p=P)
        x_rows = x.rearrange("b (t p) c -> b p t c", p=P)
        out_rows = out.rearrange("b (t p) c -> b p t c", p=P)

        def wait(eng, semaphore, value):
            if not isinstance(value, int) or value > 0:
                eng.wait_ge(semaphore, value)

        passed = sem("passed")
        bias_ready = sem("bias_ready")

        def wait_first(eng, semaphore, value):
            if not isinstance(value, int):
                eng.wait_ge(semaphore, value)
                eng.sem_inc(passed, 1)
            elif value > 0:
                eng.wait_ge(semaphore, value)

        def bank_end(t):
            return t // 2 * 2 + 2

        def h1_block(s, k):
            return h2_f32[:, TK:] if s < 2 and k == 1 else h1_f32[:]

        def of(rows, batch):
            if isinstance(batch, int):
                return rows[batch]
            return rows[bass.ds(batch, 1)].rearrange("o p t c -> p (o t) c")

        def iterations(eng, run):
            run(-1, -1, 0)
            run(0, 0, 0)
            with eng.Fori(0, PAIRS) as q:
                run(q * 2 + 1, 1, q)
                run(q * 2 + 2, 2, q)
            run(B - 1, B - 1, 0)
            run(B, B, 0)

        def has_prev(s): return s >= 1
        def has_attn(s): return 0 <= s < B
        def has_next(s): return s < B - 1
        def has_norm(s): return s < B - 1

        block = ctx.enter_context(nc.Block())

        @block.sync
        def _(sp):
            sp.dma_start(xin[:, 0], x_rows[0]).then_inc(x_loaded[0], 16)
            for cut in range(ADJ_CUTS):
                sp.dma_start(adj_rows[:, cut * CUT:(cut + 1) * CUT],
                             adj_tiles[:, cut * CUT:(cut + 1) * CUT]).then_inc(adj_loaded[cut], 16)

            sp.dma_start(xin[:, 1], x_rows[1]).then_inc(x_loaded[1], 16)

            def load(b, s):
                wait(sp, x1_made, NT * (b - 1))
                sp.dma_start(xin[:, s % 2], of(x_rows, b)).then_inc(x_loaded[s % 2], 16)

            def store(b, s):
                for k in range(NK):
                    sp.wait_ge(out_made, ELU_RING + NT * b + TK * (k + 1))
                    sp.dma_start(of(out_rows, b)[:, k * TK:(k + 1) * TK],
                                 xmid[:, s % 2, k * TK:(k + 1) * TK]).then_inc(out_stored[s % 2][k], 16)

            load(2, 2)
            with sp.Fori(0, 2) as q:
                for c in range(2):
                    load(q * 2 + c + 3, c + 3)
                    store(q * 2 + c, c)
            load(7, 7)
            store(4, 4)
            wait(sp, x1_made, NT * (B - 1))
            sp.dma_start(xin[:, 0], x_rows[B - 1]).then_inc(x_loaded[0], 16)
            for b in range(5, B):
                store(b, b)
            for parity in range(2):
                for k in range(NK):
                    sp.wait_ge(out_stored[parity][k], 16 * (B // 2))

        @block.gpsimd
        def _(pool):
            pool.memset(elu_neg[:], 0.0).then_inc(out_made, ELU_RING)
            pool.memset(ident[:], 0.0).then_inc(consts, 1)
            pool.memset(ones, 1.0).then_inc(consts, 1)
            pool.memset(neg_half[:], -0.5).then_inc(consts, 1)
            pool.wait_ge(consts, 3)
            pool.affine_select(out=ident[:], in_=ident[:], compare_op=ALU.not_equal, fill=1.0, base=0,
                               pattern=[[-1, P]], channel_multiplier=1).then_inc(consts, 1)
            pool.wait_ge(small_loaded, 16 * 5)
            pool.tensor_scalar(bias_rows[:], bias_rows[:], -1.0, None, ALU.add).then_inc(bias_ready, 1)

            def rstd_1(bb, k):
                t = slice(k * TK, (k + 1) * TK)
                n = NK * bb + k + 1
                wait_first(pool, stats1, NT * bb + TK * (k + 1))
                pool.tensor_scalar(ve1[:, t], mv1[:, t, 1], EPS, None, ALU.add).then_inc(ve1_made, 1)
                pool.wait_ge(ve1_made, n)
                pool.tensor_tensor(rs1[:, t], ve1[:, t], neg_half[:, t], ALU.pow).then_inc(rs1_made, 1)

            def norm_1(bb, k):
                t = slice(k * TK, (k + 1) * TK)
                n = NK * bb + k + 1
                pool.wait_ge(rs1_made, n)
                pool.tensor_tensor(sc1[:, t], rs1[:, t], dinv[:, t], ALU.mult).then_inc(sc1_made, 1)
                pool.wait_ge(sc1_made, n)
                pool.tensor_tensor(mr1[:, t], mv1[:, t, 0], sc1[:, t], ALU.mult).then_inc(mr1_made, 1)
                wait_first(pool, mr1_made, n)
                pool.tensor_scalar(sh1[:, t], mr1[:, t], -1.0, None, ALU.mult).then_inc(norm1, 1)

            def norm_2(bb, k):
                t = slice(k * TK, (k + 1) * TK)
                n = 3 * (NK * bb + k)
                wait_first(pool, stats2, NT * bb + TK * (k + 1))
                pool.tensor_scalar(ve2[:, t], mv2[:, t, 1], EPS, None, ALU.add).then_inc(norm2_step, 1)
                pool.wait_ge(norm2_step, n + 1)
                pool.tensor_tensor(sc2[:, t], ve2[:, t], neg_half[:, t], ALU.pow).then_inc(norm2_step, 1)
                pool.wait_ge(norm2_step, n + 2)
                pool.tensor_tensor(mr2[:, t], mv2[:, t, 0], sc2[:, t], ALU.mult).then_inc(norm2_step, 1)
                wait_first(pool, norm2_step, n + 3)
                pool.tensor_scalar(sh2[:, t], mr2[:, t], -1.0, None, ALU.mult).then_inc(norm2, 1)

            def split_1(bb, k):
                t = slice(k * TK, (k + 1) * TK)
                pool.wait_ge(h1_hi_made, NK * bb + k + 1)
                pool.tensor_tensor(h1_lo[:, t], h1_f32[:], h1_hi[:, t], ALU.subtract).then_inc(h1_split, 1)

            def split_2(bb, s, k):
                t = slice(k * TK, (k + 1) * TK)
                pool.wait_ge(h2_hi_made, NK * bb + k + 1)
                pool.tensor_tensor(h2_lo[:, s % 2, t], h2_f32[:, t], h2_hi[:, s % 2, t], ALU.subtract).then_inc(h2_split, 1)

            def add_bias(bb, s, k):
                for t in range(k * TK, (k + 1) * TK):
                    pool.wait_ge(h1_made, NT * bb + t + 1)
                    pool.tensor_tensor(xin[:, s % 2, t], xin[:, s % 2, t], bias_rows[:], ALU.add).then_inc(biased, 1)

            def output(bb, s, k):
                for t in range(k * TK, (k + 1) * TK):
                    pool.wait_ge(elu_sum, NT * bb + t + 1)
                    pool.tensor_tensor(xmid[:, s % 2, t], xmid[:, s % 2, t], elu_neg[:, t % ELU_RING], ALU.add).then_inc(out_made, 1)

            def run(b, s, q):
                attn, prev, nxt, norm = has_attn(s), has_prev(s), has_next(s), has_norm(s)
                if attn:
                    split_2(b, s, 1)
                if nxt:
                    add_bias(b + 1, s + 1, 0)
                if norm:
                    rstd_1(b + 2, 0)
                    norm_1(b + 2, 0)
                if s < 0:
                    rstd_1(b + 2, 1)
                    norm_1(b + 2, 1)
                if prev:
                    output(b - 1, s - 1, 0)
                if nxt:
                    add_bias(b + 1, s + 1, 1)
                    norm_2(b + 1, 0)
                    split_2(b + 1, s + 1, 0)
                if prev:
                    output(b - 1, s - 1, 1)
                if norm and s >= 0:
                    rstd_1(b + 2, 1)
                    norm_1(b + 2, 1)
                    split_1(b + 2, 0)
                if nxt:
                    norm_2(b + 1, 1)
                if norm and s >= 0:
                    split_1(b + 2, 1)

            for k in range(NK):
                rstd_1(0, k)
            pool.wait_ge(deg_even, ADJ_CUTS)
            pool.wait_ge(deg_odd, ADJ_CUTS)
            pool.tensor_scalar(deg_pos[:], deg[:], 0.0, None, ALU.is_gt).then_inc(dinv_made, 1)
            pool.tensor_scalar(dinv_out[:], deg[:], 1.2e-38, None, ALU.max).then_inc(dinv_made, 1)
            pool.wait_ge(dinv_made, 2)
            pool.tensor_tensor(dinv[:], dinv_out[:], neg_half[:], ALU.pow).then_inc(dinv_made, 1)
            pool.wait_ge(dinv_made, 3)
            pool.tensor_tensor(dinv[:], dinv[:], deg_pos[:], ALU.mult).then_inc(dinv_made, 1)
            pool.wait_ge(dinv_made, 4)
            for k in range(NK):
                norm_1(0, k)
            pool.tensor_scalar(dinv_out[:], dinv[:], 1.0 / (ADJ_SCALE * W_SCALE), None, ALU.mult).then_inc(dinv_made, 1)
            pool.wait_ge(bias_ready, 1)
            iterations(pool, run)

        @block.scalar
        def _(act):
            act.dma_start(w0_raw, w0.rearrange("(k p) c -> p k c", p=P)).then_inc(small_loaded, 16)
            act.dma_start(w1_raw, w1.rearrange("(k p) c -> p k c", p=P)).then_inc(small_loaded, 16)
            act.dma_start(a_cols[:], a.rearrange("(k p) o -> p (k o)", p=P), allow_slow_non_contiguous=True).then_inc(small_loaded, 16)
            act.dma_start(bias_rows[:], bias.rearrange("(o c) -> o c", o=1).broadcast_to([P, C])).then_inc(small_loaded, 16)
            act.dma_start(beta_col[:], beta.rearrange("(o c) -> o c", o=1).broadcast_to([P, 1])).then_inc(small_loaded, 16)
            for cut in range(ADJ_CUTS):
                even = cut * CUT
                act.wait_ge(adj_loaded[cut], 16)
                if cut >= 2:
                    act.wait_ge(deg_even, cut - 1)
                act.activation(score[:, 2 + cut % 2], adj_rows[:, even], ACT.Copy,
                               accum_out=deg[:, even:even + 1]).then_inc(deg_even, 1)
                for n in range(even, even + CUT):
                    act.wait_ge(adjT_tr, n + 1)
                    act.activation(adjT_hi[:, :, n * P:(n + 1) * P], tr_ps[:, n % 2].rearrange("p (m i) -> p m i", m=NT),
                                   ACT.Copy, scale=ADJ_SCALE).then_inc(adjT_hi_made, 1)
            def relu_1(bb, s, k):
                act.wait_ge(norm1, NK * bb + k + 1)
                if s < 2:
                    wait(act, h1_split, NK * bb)
                else:
                    act.wait_ge(h1_split, NK * bb + k)
                for i in range(TK):
                    n = k * TK + i
                    act.activation(h1_block(s, k)[:, i], xin[:, s % 2, n], ACT.Relu, bias=sh1[:, n:n + 1],
                                   scale=sc1[:, n:n + 1]).then_inc(h1_made, 1)

            def hi_1(bb, s, k):
                t = slice(k * TK, (k + 1) * TK)
                wait(act, u_done, GROUPS * bb)
                act.wait_ge(h1_made, NT * bb + TK * (k + 1))
                act.activation(h1_hi[:, t], h1_block(s, k), ACT.Copy).then_inc(h1_hi_made, 1)

            def relu_2(bb, s, k):
                act.wait_ge(norm2, NK * bb + k + 1)
                wait(act, dots, 2 * (NT * (bb - 1) + TK * (k + 1)))
                wait(act, h2_split, NK * (bb - 1) + k + 1)
                if s == 0 and k == 1:
                    act.wait_ge(h1_split, 2 * NK)
                for n in range(k * TK, (k + 1) * TK):
                    act.activation(h2_f32[:, n], xmid[:, s % 2, n], ACT.Relu, bias=sh2[:, n:n + 1],
                                   scale=sc2[:, n:n + 1]).then_inc(h2_made, 1)

            def hi_2(bb, s, k):
                t = slice(k * TK, (k + 1) * TK)
                wait(act, v_done, GROUPS * (bb - 1))
                act.wait_ge(h2_made, NT * bb + TK * (k + 1))
                act.activation(h2_hi[:, s % 2, t], h2_f32[:, t], ACT.Copy).then_inc(h2_hi_made, 1)

            def keep_s2(b, s):
                wait(act, leaky, NT * b)
                act.wait_ge(s2_done, b + 1)
                act.activation(s2_rows[:], tr_ps[:, s % 2], ACT.Copy).then_inc(s2_made, 1)

            def relu(b, s, t):
                if t == 0:
                    act.wait_ge(dots4, NK * b + NK)
                    act.wait_ge(s2_made, b + 1)
                wait(act, p_tr, NT * b + t + 1 - RING)
                act.activation(score[:, t % RING], s2_rows[:], ACT.Relu, bias=s1_col4[:, s % 2, t:t + 1],
                               scale=4.0).then_inc(relu_made, 1)

            def exp(b, s, t):
                act.wait_ge(neg_max_made, NT * b + t + 1)
                act.activation(score[:, t % RING], score[:, t % RING], ACT.Exp, bias=neg_max[:, t:t + 1],
                               scale=SLOPE, accum_out=row_sum[:, s % 2, t:t + 1]).then_inc(exp_made, 1)

            def hi_pT(b, s, t):
                k = t // TK
                if t % TK == 0:
                    wait(act, v_done, GROUPS * (b - 1) + CT * (k + 1))
                act.wait_ge(p_tr, NT * b + t + 1)
                act.activation(pT_hi[:, k, :, (t % TK) * P:(t % TK + 1) * P],
                               tr_ps[:, (s + t + 1) % 2].rearrange("p (j i) -> p j i", j=NT),
                               ACT.Copy).then_inc(pT_hi_made, 1)

            def hi_u(bb, g):
                wait(act, p0_done, NT * bb + TK * (g // CT))
                act.wait_ge(u_done, GROUPS * bb + g + 1)
                act.activation(u_hi[:, g % CT], mix_ps[:, g % 2], ACT.Copy).then_inc(u_hi_made, 1)

            def hi_v(bb, g):
                wait(act, p1_done, NT * bb + TK * (g // CT))
                act.wait_ge(v_done, GROUPS * bb + g + 1)
                act.activation(v_hi[:, g % CT], mix_ps[:, g % 2], ACT.Copy).then_inc(v_hi_made, 1)

            def elu(bb, s, k, half):
                if half == 0:
                    act.wait_ge(inv_made, NK * bb + k + 1)
                for t in range(k * TK + 2 * half, k * TK + 2 * half + 2):
                    act.wait_ge(out_made, ELU_RING + NT * bb + t + 1 - ELU_RING)
                    act.wait_ge(p1_done, NT * bb + bank_end(t))
                    inv = inv_sum[:, s % 2, t:t + 1]
                    act.activation(elu_neg[:, t % ELU_RING], proj_ps[:, t % TK], ACT.Exp, scale=inv).then_inc(elu_exp, 1)
                    act.activation(elu_pos[:, t % ELU_RING], proj_ps[:, t % TK], ACT.Relu, scale=inv).then_inc(elu_relu, 1)

            def run(b, s, q):
                attn, prev, nxt, norm = has_attn(s), has_prev(s), has_next(s), has_norm(s)
                if prev:
                    hi_v(b - 1, 1)
                    hi_pT(b - 1, s - 1, 6)
                if attn:
                    relu_2(b, s, 1)
                    hi_2(b, s, 1)
                if nxt:
                    hi_u(b + 1, 0)
                if prev:
                    hi_pT(b - 1, s - 1, 7)
                if attn:
                    keep_s2(b, s)
                    relu(b, s, 0)
                    relu(b, s, 1)
                if prev:
                    elu(b - 1, s - 1, 0, 0)
                if attn:
                    exp(b, s, 0)
                    relu(b, s, 2)
                if prev:
                    elu(b - 1, s - 1, 0, 1)
                if nxt:
                    hi_u(b + 1, 1)
                if attn:
                    exp(b, s, 1)
                    hi_pT(b, s, 0)
                    relu(b, s, 3)
                    exp(b, s, 2)
                if prev:
                    hi_v(b - 1, 2)
                if attn:
                    hi_pT(b, s, 1)
                    relu(b, s, 4)
                    exp(b, s, 3)
                    relu(b, s, 5)
                if prev:
                    hi_v(b - 1, 3)
                if nxt:
                    relu_2(b + 1, s + 1, 0)
                if attn:
                    hi_pT(b, s, 2)
                    exp(b, s, 4)
                if nxt:
                    hi_u(b + 1, 2)
                    hi_2(b + 1, s + 1, 0)
                if attn:
                    relu(b, s, 6)
                    hi_pT(b, s, 3)
                    exp(b, s, 5)
                if norm:
                    relu_1(b + 2, s + 2, 0)
                if prev:
                    elu(b - 1, s - 1, 1, 0)
                if attn:
                    relu(b, s, 7)
                if prev:
                    elu(b - 1, s - 1, 1, 1)
                if nxt:
                    hi_u(b + 1, 3)
                if attn:
                    exp(b, s, 6)
                    hi_pT(b, s, 4)
                if norm:
                    hi_1(b + 2, s + 2, 0)
                if attn:
                    hi_v(b, 0)
                    exp(b, s, 7)
                    hi_pT(b, s, 5)
                if norm:
                    relu_1(b + 2, s + 2, 1)
                    hi_1(b + 2, s + 2, 1)

            for k in range(NK):
                relu_1(0, 0, k)
                hi_1(0, 0, k)
            act.wait_ge(small_loaded, 16 * 5)
            act.activation(w0_hi[:], w0_raw, ACT.Copy, scale=W_SCALE).then_inc(w_scaled, 1)
            act.activation(w1_hi[:], w1_raw, ACT.Copy, scale=W_SCALE).then_inc(w_scaled, 1)
            iterations(act, run)

        @block.tensor
        def _(pe):
            def product(dst, left, right, first, last):
                pe.matmul(dst, left[0], right[0], start=first, stop=False)
                pe.matmul(dst, left[0], right[1], start=False, stop=False)
                return pe.matmul(dst, left[1], right[0], start=False, stop=last)

            pe.wait_ge(consts, 4)
            for n in range(NT):
                pe.wait_ge(adj_loaded[n // CUT], 16)
                if n >= 2:
                    pe.wait_ge(adjT_lo_made, n - 1)
                for m in range(NT):
                    mm = pe.transpose(tr_ps[:, n % 2, m * P:(m + 1) * P], adj_rows[:, n, m * P:(m + 1) * P], ident[:])
                mm.then_inc(adjT_tr, 1)

            pe.wait_ge(small_loaded, 16 * 5)
            for k in range(CT):
                for f in range(CT):
                    mm = pe.transpose(proj_ps[:, f, k * P:(k + 1) * P], w1_raw[:, k, f * P:(f + 1) * P], ident[:])
            mm.then_inc(wT_tr, 1)
            pe.wait_ge(wT_made, 1)
            pe.wait_ge(wide_made, 4)
            for i in range(2):
                for f in range(CT):
                    mm = pe.matmul(proj_ps[:, 2 + i], a_wide[:, i * CT + f], w1T[:, f], start=f == 0, stop=f == CT - 1)
            mm.then_inc(wa_done, 1)

            def mix_u(bb, g):
                k, c = g // CT, g % CT
                cols = slice(c * P, (c + 1) * P)
                rows = slice(k * HALF, (k + 1) * HALF)
                for m in range(NT):
                    if g == 0 and m % TK == 0:
                        pe.wait_ge(h1_split, NK * bb + m // TK + 1)
                    mm = product(mix_ps[:, g % 2], (h1_hi[:, m, cols], h1_lo[:, m, cols]),
                                 (adjT_hi[:, m, rows], adjT_lo[:, m, rows]), m == 0, m == NT - 1)
                mm.then_inc(u_done, 1)

            def mix_v(bb, s, g):
                k, c = g // CT, g % CT
                cols = slice(c * P, (c + 1) * P)
                pe.wait_ge(pT_split, NT * bb + TK * (k + 1))
                for m in range(NT):
                    if g == 0 and m % TK == 0:
                        pe.wait_ge(h2_split, NK * bb + m // TK + 1)
                    mm = product(mix_ps[:, g % 2], (h2_hi[:, s % 2, m, cols], h2_lo[:, s % 2, m, cols]),
                                 (pT_hi[:, k, m], pT_lo[:, k, m]), m == 0, m == NT - 1)
                mm.then_inc(v_done, 1)

            def project(left_hi, left_lo, w_hi, w_lo, i, done):
                rows = slice(i * P, (i + 1) * P)
                for c in range(CT):
                    mm = product(proj_ps[:, i], (left_hi[:, c, rows], left_lo[:, c, rows]),
                                 (w_hi[:, c], w_lo[:, c]), c == 0, c == CT - 1)
                mm.then_inc(done, 1)

            def project_u(bb, s, k):
                pe.wait_ge(u_split, GROUPS * bb + CT * (k + 1))
                for i in range(TK):
                    if s >= 2:
                        pe.wait_ge(elu_relu, NT * (bb - 2) + TK * k + bank_end(i))
                    else:
                        wait(pe, x1_made, NT * bb + TK * (k - 1) + bank_end(i))
                    project(u_hi, u_lo, w0_hi, w0_lo, i, p0_done)

            def project_v(bb, s, k):
                pe.wait_ge(v_split, GROUPS * bb + CT * (k + 1))
                for i in range(TK):
                    if s + 1 + k < B:
                        pe.wait_ge(x1_made, NT * (bb + 1) + TK + TK * k + bank_end(i))
                    else:
                        pe.wait_ge(elu_relu, NT * bb + TK * (k - 1) + bank_end(i))
                    project(v_hi, v_lo, w1_hi, w1_lo, i, p1_done)

            def spread_s2(b, s):
                wait(pe, pT_split, NT * b - 1)
                pe.wait_ge(dots, 2 * NT * (b + 1))
                for t in range(NT):
                    mm = pe.transpose(tr_ps[:, s % 2, t * P:(t + 1) * P], s2_col[:, t:t + 1].broadcast_to([P, P]), ident[:])
                mm.then_inc(s2_done, 1)

            def transpose_p(b, s, t):
                if t == 1:
                    pe.wait_ge(s2_made, b + 1)
                else:
                    wait(pe, pT_split, NT * b + t - 1 if t else NT * b)
                pe.wait_ge(p_made, NT * b + t + 1)
                for j in range(NT):
                    mm = pe.transpose(tr_ps[:, (s + t + 1) % 2, j * P:(j + 1) * P],
                                      score[:, t % RING, j * P:(j + 1) * P], ident[:])
                mm.then_inc(p_tr, 1)

            def run(b, s, q):
                attn, prev, nxt = has_attn(s), has_prev(s), has_next(s)
                if nxt:
                    if prev:
                        pe.wait_ge(v_split, GROUPS * (b - 1) + 1)
                    else:
                        wait(pe, u_split, GROUPS * b + 3)
                    mix_u(b + 1, 0)
                if prev:
                    transpose_p(b - 1, s - 1, 7)
                if attn and prev:
                    spread_s2(b, s)
                if prev:
                    project_v(b - 1, s - 1, 0)
                if nxt:
                    if prev:
                        pe.wait_ge(v_split, GROUPS * (b - 1) + 2)
                    else:
                        wait(pe, u_split, GROUPS * b + 4)
                    mix_u(b + 1, 1)
                if s < 0:
                    pe.wait_ge(w_split, 2)
                    pe.wait_ge(wa_made, 1)
                    pe.wait_ge(adjT_lo_made, NT)
                if s == 0:
                    spread_s2(b, s)
                if attn and nxt:
                    transpose_p(b, s, 0)
                if prev:
                    if nxt:
                        pe.wait_ge(u_split, GROUPS * (b + 1) + 1)
                    else:
                        pe.wait_ge(v_split, GROUPS * (b - 1) + 1)
                    mix_v(b - 1, s - 1, 2)
                if attn:
                    if not nxt:
                        transpose_p(b, s, 0)
                    transpose_p(b, s, 1)
                if nxt:
                    project_u(b + 1, s + 1, 0)
                if prev:
                    if nxt:
                        pe.wait_ge(u_split, GROUPS * (b + 1) + 2)
                    else:
                        pe.wait_ge(v_split, GROUPS * (b - 1) + 2)
                    mix_v(b - 1, s - 1, 3)
                if attn:
                    transpose_p(b, s, 2)
                if nxt:
                    if prev:
                        pe.wait_ge(v_split, GROUPS * (b - 1) + 3)
                    else:
                        pe.wait_ge(u_split, GROUPS * (b + 1) + 1)
                    mix_u(b + 1, 2)
                if attn:
                    transpose_p(b, s, 3)
                if prev:
                    project_v(b - 1, s - 1, 1)
                if nxt:
                    if prev:
                        pe.wait_ge(v_split, GROUPS * (b - 1) + 4)
                    else:
                        pe.wait_ge(u_split, GROUPS * (b + 1) + 2)
                    mix_u(b + 1, 3)
                if attn:
                    transpose_p(b, s, 4)
                    if nxt:
                        pe.wait_ge(u_split, GROUPS * (b + 1) + 3)
                    else:
                        pe.wait_ge(v_split, GROUPS * (b - 1) + 3)
                    mix_v(b, s, 0)
                    transpose_p(b, s, 5)
                if nxt:
                    project_u(b + 1, s + 1, 1)
                if attn:
                    if nxt:
                        pe.wait_ge(u_split, GROUPS * (b + 1) + 4)
                    else:
                        pe.wait_ge(v_split, GROUPS * (b - 1) + 4)
                    mix_v(b, s, 1)
                    transpose_p(b, s, 6)

            pe.wait_ge(adjT_lo_made, TK)
            iterations(pe, run)

        @block.vector
        def _(dve):
            def stats_1(bb, s, q, k):
                dve.wait_ge(x_loaded[s % 2], (q + s // 2) * 16 + 16)
                for t in range(k * TK, (k + 1) * TK):
                    dve.bn_stats(st1[:, t], xin[:, s % 2, t]).then_inc(bn1, 1)
                wait_first(dve, bn1, NT * bb + TK * (k + 1))
                for t in range(k * TK, (k + 1) * TK):
                    dve.bn_aggr(mv1[:, t], st1[:, t]).then_inc(stats1, 1)

            def split_1(bb, s, k):
                dve.wait_ge(h1_hi_made, NK * bb + k + 1)
                dve.tensor_tensor(h1_lo[:, k * TK:(k + 1) * TK], h1_block(s, k), h1_hi[:, k * TK:(k + 1) * TK],
                                  ALU.subtract).then_inc(h1_split, 1)

            stats_1(0, 0, 0, 0)
            stats_1(0, 0, 0, 1)
            def degree(cut):
                odd = cut * CUT + 1
                dve.wait_ge(adj_loaded[cut], 16)
                dve.reduce_sum(deg[:, odd:odd + 1], adj_rows[:, odd], AX.X).then_inc(deg_odd, 1)

            def lo_adjT(n):
                dve.wait_ge(adjT_hi_made, n + 1)
                dve.scalar_tensor_tensor(adjT_lo[:, :, n * P:(n + 1) * P], tr_ps[:, n % 2].rearrange("p (m i) -> p m i", m=NT),
                                         ADJ_SCALE, adjT_hi[:, :, n * P:(n + 1) * P], ALU.mult,
                                         ALU.subtract).then_inc(adjT_lo_made, 1)

            for cut in range(ADJ_CUTS):
                degree(cut)
                for n in range(cut * CUT, (cut + 1) * CUT):
                    lo_adjT(n)
            dve.wait_ge(small_loaded, 16 * 5)
            dve.wait_ge(consts, 4)
            for i in range(2 * CT):
                dve.tensor_scalar(a_wide[:, i], ones, a_cols[:, i:i + 1], None, ALU.mult).then_inc(wide_made, 1)
            dve.wait_ge(wT_tr, 1)
            dve.tensor_copy(w1T, proj_ps[:, 0:CT]).then_inc(wT_made, 1)
            dve.tensor_scalar(beta_ident[:], ident[:], beta_col[:, 0:1], None, ALU.mult).then_inc(beta_ready, 1)
            dve.wait_ge(beta_ready, 1)
            split_1(0, 0, 0)
            dve.wait_ge(wa_done, 1)
            dve.tensor_copy(wa_rows[:], proj_ps[:, 2:4]).then_inc(wa_made, 1)
            split_1(0, 0, 1)
            dve.wait_ge(w_scaled, 2)
            dve.scalar_tensor_tensor(w0_lo[:], w0_raw, W_SCALE, w0_hi[:], ALU.mult, ALU.subtract).then_inc(w_split, 1)
            dve.scalar_tensor_tensor(w1_lo[:], w1_raw, W_SCALE, w1_hi[:], ALU.mult, ALU.subtract).then_inc(w_split, 1)

            def x1_stats_2(bb, s, q, k):
                tiles = range(k * TK, (k + 1) * TK)
                wait(dve, out_stored[s % 2][k], (q + s // 2) * 16)
                for t in tiles:
                    dve.wait_ge(biased, NT * bb + t + 1)
                    dve.wait_ge(p0_done, NT * bb + bank_end(t))
                    dve.scalar_tensor_tensor(xmid[:, s % 2, t], proj_ps[:, t % TK], dinv_out[:, t:t + 1],
                                             xin[:, s % 2, t], ALU.mult, ALU.add).then_inc(x1_made, 1)
                for t in tiles:
                    dve.wait_ge(x1_made, NT * bb + t + 1)
                    dve.bn_stats(st2[:, t], xmid[:, s % 2, t]).then_inc(bn2, 1)
                wait_first(dve, bn2, NT * bb + TK * (k + 1))
                for t in tiles:
                    dve.bn_aggr(mv2[:, t], st2[:, t]).then_inc(stats2, 1)

            def dots_2(bb, s, k):
                wait(dve, s2_done, bb)
                for t in range(k * TK, (k + 1) * TK):
                    for i, col in enumerate((s1_col[:, s % 2, t:t + 1], s2_col[:, t:t + 1])):
                        wait(dve, dots, 2 * (NT * bb + t) + i - 1)
                        if i == 0:
                            dve.wait_ge(h2_made, NT * bb + t + 1)
                        dve.tensor_tensor_reduce(dots_out[:, i], h2_f32[:, t], wa_rows[:, i], 1.0, 0.0, ALU.mult,
                                                 ALU.add, col).then_inc(dots, 1)
                wait(dve, dots, 2 * (NT * bb + TK * (k + 1)))
                dve.tensor_scalar(s1_col4[:, s % 2, k * TK:(k + 1) * TK], s1_col[:, s % 2, k * TK:(k + 1) * TK],
                                  4.0, None, ALU.mult).then_inc(dots4, 1)

            def leaky_relu(b, s, t):
                dve.wait_ge(relu_made, NT * b + t + 1)
                dve.scalar_tensor_tensor(score[:, t % RING], s2_rows[:], s1_col[:, s % 2, t:t + 1], score[:, t % RING],
                                         ALU.add, ALU.add).then_inc(leaky, 1)

            def mask_max(b, s, t):
                wait_first(dve, leaky, NT * b + t + 1)
                dve.tensor_tensor_reduce(score[:, t % RING], score[:, t % RING], adj_rows[:, t], 1.0, LOWEST, ALU.mult,
                                         ALU.max, max5[:, t:t + 1]).then_inc(masked, 1)
                dve.wait_ge(masked, NT * b + t + 1)
                dve.tensor_scalar(neg_max[:, t:t + 1], max5[:, t:t + 1], -SLOPE, None, ALU.mult).then_inc(neg_max_made, 1)

            def add_beta(b, s, t):
                dve.wait_ge(exp_made, NT * b + t + 1)
                diag = score[:, t % RING, t * P:(t + 1) * P]
                dve.scalar_tensor_tensor(diag, beta_ident[:], row_sum[:, s % 2, t:t + 1], diag, ALU.mult, ALU.add).then_inc(p_made, 1)

            def invert_sums(b, s, k):
                t = slice(k * TK, (k + 1) * TK)
                dve.tensor_scalar(sum_scaled[:, t], row_sum[:, s % 2, t], W_SCALE, None, ALU.mult).then_inc(scaled, 1)
                dve.wait_ge(scaled, NK * b + k + 1)
                dve.reciprocal(inv_sum[:, s % 2, t], sum_scaled[:, t]).then_inc(inv_made, 1)

            def lo_pT(b, s, t):
                k = t // TK
                cols = slice((t % TK) * P, (t % TK + 1) * P)
                dve.wait_ge(pT_hi_made, NT * b + t + 1)
                dve.scalar_tensor_tensor(pT_lo[:, k, :, cols], tr_ps[:, (s + t + 1) % 2].rearrange("p (j i) -> p j i", j=NT),
                                         1.0, pT_hi[:, k, :, cols], ALU.mult, ALU.subtract).then_inc(pT_split, 1)

            def lo_u(bb, g):
                dve.wait_ge(u_hi_made, GROUPS * bb + g + 1)
                dve.scalar_tensor_tensor(u_lo[:, g % CT], mix_ps[:, g % 2], 1.0, u_hi[:, g % CT],
                                         ALU.mult, ALU.subtract).then_inc(u_split, 1)

            def lo_v(bb, g):
                dve.wait_ge(v_hi_made, GROUPS * bb + g + 1)
                dve.scalar_tensor_tensor(v_lo[:, g % CT], mix_ps[:, g % 2], 1.0, v_hi[:, g % CT],
                                         ALU.mult, ALU.subtract).then_inc(v_split, 1)

            def elu_sums(bb, k, half):
                for t in range(k * TK + 2 * half, k * TK + 2 * half + 2):
                    dve.wait_ge(elu_relu, NT * bb + t + 1)
                    dve.scalar_tensor_tensor(elu_neg[:, t % ELU_RING], elu_neg[:, t % ELU_RING], 1.0,
                                             elu_pos[:, t % ELU_RING], ALU.min, ALU.add).then_inc(elu_sum, 1)

            def run(b, s, q):
                attn, prev, nxt, norm = has_attn(s), has_prev(s), has_next(s), has_norm(s)
                if prev:
                    lo_v(b - 1, 1)
                    lo_pT(b - 1, s - 1, 6)
                if attn:
                    dots_2(b, s, 1)
                if nxt:
                    lo_u(b + 1, 0)
                if prev:
                    lo_pT(b - 1, s - 1, 7)
                if norm:
                    stats_1(b + 2, s + 2, q, 0)
                if s < 0:
                    stats_1(b + 2, s + 2, q, 1)
                if attn:
                    leaky_relu(b, s, 0)
                    mask_max(b, s, 0)
                if prev:
                    elu_sums(b - 1, 0, 0)
                if attn:
                    leaky_relu(b, s, 1)
                    add_beta(b, s, 0)
                    mask_max(b, s, 1)
                if prev:
                    elu_sums(b - 1, 0, 1)
                if nxt:
                    lo_u(b + 1, 1)
                if attn:
                    leaky_relu(b, s, 2)
                    add_beta(b, s, 1)
                    mask_max(b, s, 2)
                    leaky_relu(b, s, 3)
                    lo_pT(b, s, 0)
                    mask_max(b, s, 3)
                    add_beta(b, s, 2)
                if prev:
                    lo_v(b - 1, 2)
                if attn:
                    lo_pT(b, s, 1)
                if nxt:
                    x1_stats_2(b + 1, s + 1, q, 0)
                if attn:
                    leaky_relu(b, s, 4)
                    mask_max(b, s, 4)
                    add_beta(b, s, 3)
                    invert_sums(b, s, 0)
                if prev:
                    lo_v(b - 1, 3)
                if attn:
                    leaky_relu(b, s, 5)
                    lo_pT(b, s, 2)
                    mask_max(b, s, 5)
                    add_beta(b, s, 4)
                if nxt:
                    lo_u(b + 1, 2)
                    dots_2(b + 1, s + 1, 0)
                if attn:
                    lo_pT(b, s, 3)
                if prev:
                    elu_sums(b - 1, 1, 0)
                if attn:
                    leaky_relu(b, s, 6)
                    mask_max(b, s, 6)
                    add_beta(b, s, 5)
                if prev:
                    elu_sums(b - 1, 1, 1)
                if nxt:
                    lo_u(b + 1, 3)
                if s < 0:
                    split_1(b + 2, s + 2, 0)
                    split_1(b + 2, s + 2, 1)
                elif norm:
                    stats_1(b + 2, s + 2, q, 1)
                if attn:
                    leaky_relu(b, s, 7)
                    mask_max(b, s, 7)
                    add_beta(b, s, 6)
                    lo_pT(b, s, 4)
                    lo_v(b, 0)
                if nxt:
                    x1_stats_2(b + 1, s + 1, q, 1)
                if attn:
                    lo_pT(b, s, 5)
                    add_beta(b, s, 7)
                    invert_sums(b, s, 1)

            dve.wait_ge(dinv_made, 5)
            dve.wait_ge(wa_made, 1)
            iterations(dve, run)


_INS = ["x", "adj", "L0_gnn_weight", "L0_gnn_bias", "L1_gnn_W", "L1_gnn_a", "L1_gnn_beta"]


def kernel(**inputs):
    import numpy as np
    import concourse.bacc as bacc
    from concourse.bass_utils import run_bass_kernel_spmd

    nc = bacc.Bacc("TRN2", target_bir_lowering=False, num_devices=1)
    arrays, args = {}, []
    for name in _INS:
        a = np.ascontiguousarray(inputs[name])
        arrays["in_" + name] = a
        args.append(nc.dram_tensor("in_" + name, a.shape, mybir.dt.from_np(a.dtype), kind="ExternalInput").ap())
    args.append(nc.dram_tensor("out_x", inputs["x"].shape, F32, kind="ExternalOutput").ap())
    two_layers(nc, *args)
    r = run_bass_kernel_spmd(nc, [arrays], core_ids=[0])
    return r.results[0]["out_x"]
```
